# Optimizing a Trainium2 kernel written in Bass

```python
import numpy as np
import jax
import jax.numpy as jnp

def _softmax(x, axis=-1):
    return jax.nn.softmax(x, axis=axis)

def _gelu(x):
    return jax.nn.gelu(x, approximate=True)

def _silu(x):
    return jax.nn.silu(x)

def _sigmoid(x):
    return jax.nn.sigmoid(x)

def _layernorm(x, axis=-1, eps=1e-05):
    m = jnp.mean(x, axis=axis, keepdims=True)
    v = jnp.var(x, axis=axis, keepdims=True)
    return (x - m) / jnp.sqrt(v + eps)

def _scatter_add(tgt, idx, src, axis=0):
    return tgt.at[idx].add(src)

def _segment_sum(src, seg, n):
    return jax.ops.segment_sum(src, seg, n)
kernel_name = 'mk_rec_standalone_d1_rec_r8_72f151'

def setup_inputs(seed: int=0):
    np.random.seed(seed)
    _w = jnp.asarray

    def _rec_inputs():
        import jax
        import jax.numpy as jnp
        _rk = jax.random.key(seed)
        r_feature_emb = -0.000292821 + 1.00034 * jax.random.normal(jax.random.fold_in(_rk, 1), (2048, 32, 64), jnp.float32)
        return r_feature_emb
    r_feature_emb = _rec_inputs()

    def _L0_rec_setup():
        import jax, jax.numpy as jnp
        import numpy as np
        from itertools import combinations
        NUM_FIELDS = 32
        EMB_DIM = 64
        BATCH = 256
        PAIRS = np.array(list(combinations(range(NUM_FIELDS), 2)), dtype=np.int32)
        key = jax.random.key(seed)
        k1, k2 = jax.random.split(key)
        feature_emb = jax.random.normal(k1, (BATCH, NUM_FIELDS, EMB_DIM), dtype=jnp.float32)
        P = PAIRS.shape[0]
        bound = float(np.sqrt(6.0 / (EMB_DIM + EMB_DIM)))
        W = jax.random.uniform(k2, (P, EMB_DIM, EMB_DIM), minval=-bound, maxval=bound, dtype=jnp.float32)
        return {'feature_emb': feature_emb, 'W': W}
    _L0_rec_all = _L0_rec_setup()
    _L0_rec_in = {k: v for k, v in _L0_rec_all.items() if k in ('W',)}
    del _L0_rec_all
    return {'r_feature_emb': r_feature_emb, 'L0_rec_W': _L0_rec_in['W']}

def reference(r_feature_emb, L0_rec_W):
    import jax
    import jax.numpy as jnp

    def _L0_rec_ref(feature_emb, W):
        import jax, jax.numpy as jnp
        import numpy as np
        from itertools import combinations
        NUM_FIELDS = 32
        EMB_DIM = 64
        BATCH = 256
        PAIRS = np.array(list(combinations(range(NUM_FIELDS), 2)), dtype=np.int32)
        idx_i = jnp.asarray(PAIRS[:, 0])
        idx_j = jnp.asarray(PAIRS[:, 1])
        v_i = feature_emb[:, idx_i, :]
        v_j = feature_emb[:, idx_j, :]
        proj = jnp.einsum('bpd,ped->bpe', v_i, W)
        return proj * v_j
    y = _L0_rec_ref(r_feature_emb, L0_rec_W)
    return y

_drawn_inputs = setup_inputs


def setup_inputs(seed=0):
    import zlib

    import numpy as np

    out = dict(_drawn_inputs(seed))
    spreads = {}
    factors = {}
    for name, (base, spread) in spreads.items():
        noise = np.random.default_rng([zlib.crc32(name.encode()), seed]).standard_normal(out[name].shape)
        drawn = base * np.exp(spread * noise) if base else spread * noise
        out[name] = jnp.asarray(drawn.astype(out[name].dtype))
    for name, factor in factors.items():
        out[name] = (out[name] * factor).astype(out[name].dtype)
    return out
```

```python
from contextlib import ExitStack
from math import ceil

import concourse.bass as bass
from concourse import mybir

ALU = mybir.AluOpType
F32 = mybir.dt.float32
F32R = mybir.dt.float32r

P = 128
TILES = 2
BANK = 512
UNITS = 3
N_RING = 2
T_RING = 2
S_RING = 4
AHEAD = 2
OUT_RING = 4
OUT_PAIRS = 16
W_ROWS = 8
W_STAGES = 4
W_SPLITS = 2
W_STEP = 2


def cut_groups(fields, bank_pairs):
    groups = []
    for i in range(fields - 1):
        left = fields - 1 - i
        if left == 1:
            groups[-1].append((i, i + 1, 1))
            continue
        n, j = ceil(left / bank_pairs), i + 1
        for k in range(n):
            size = left // n + (k < left % n)
            groups.append([(i, j, size)])
            j += size
    return groups


def cut_chunks(sizes, most):
    chunks, held = [[]], 0
    for g, size in enumerate(sizes):
        if held + size > most:
            chunks.append([])
            held = 0
        chunks[-1].append(g)
        held += size
    return chunks


def last_user(k, ring, count):
    return max(n for n in range(count) if n % ring == k % ring)


def bilinear_interaction(nc, emb, w, out):
    B, F, D = emb.shape
    NP = w.shape[0]
    SUPER = B // (TILES * P)
    NF = F - 1
    NQ = F // 2
    groups = cut_groups(F, BANK // D)
    NG = len(groups)
    sizes = [sum(n for _, _, n in g) for g in groups]
    first_pair = [sum(sizes[:g]) for g in range(NG)]
    chunks = cut_chunks(sizes, OUT_PAIRS)
    NC = len(chunks)
    chunk_of = {g: c for c, gs in enumerate(chunks) for g in gs}
    groups_of = [[g for g in range(NG) if groups[g][-1][0] == i] for i in range(NF)]
    groups_through = [sum(g[0][0] <= i for g in groups) for i in range(NF)]

    W_PAIRS = W_ROWS * P // D
    NW = NP // W_PAIRS
    W_TURNS = W_ROWS * P // BANK
    TURNS = BANK // P
    w_by = [min(NW, max(ceil((i + 1) * (2 * F - 2 - i) / 2 / W_PAIRS), W_STEP * (i + 1))) for i in range(NF)]
    w_before = [list(range(w_by[i - 1] if i else 0, w_by[i])) for i in range(NF)]
    W_DONE = w_by.index(NW)

    assert NP == F * (F - 1) // 2 and 2 * D == P and B % (2 * TILES * P) == 0 and SUPER >= 4
    assert NC % OUT_RING == 0 and NF % 2 == 1 and NQ % N_RING == 0 and 2 * TILES == TURNS
    assert T_RING == 2 and W_TURNS % 2 == 0 and NP % W_PAIRS == 0 and W_DONE + S_RING < NF
    assert w_by[-1] == NW and W_SPLITS <= W_STAGES < NW

    emb_rows = emb.rearrange("(s t p) f d -> s p t (f d)", t=TILES, p=P)
    out_rows = out.rearrange("(s t p) n e -> s p t (n e)", t=TILES, p=P)
    w_rows = w.rearrange("n e d -> (n e d)").rearrange("(k x m) -> k x m", x=P, m=W_ROWS * D)

    with ExitStack() as ctx:
        def sb(name, shape, dt=F32):
            return ctx.enter_context(nc.sbuf_tensor(name, shape, dt))

        def sem(name):
            return ctx.enter_context(nc.semaphore(name))

        w_split = sb("w_split", [P, NP * D], F32R)
        v = [sb(f"v{b}", [P, TILES, F * D]) for b in range(2)]
        n_split = sb("n_split", [P, N_RING, TILES, 2, 3 * D], F32R)
        s_split = sb("s_split", [P, S_RING, 2 * TILES, P], F32R)
        out_chunk = sb("out_chunk", [P, OUT_RING, TILES, OUT_PAIRS * D])
        identity = sb("identity", [P, P])
        proj = ctx.enter_context(nc.psum_tensor("proj", [P, UNITS, TILES, BANK], F32))
        turned = ctx.enter_context(nc.psum_tensor("turned", [P, T_RING, TURNS, P], F32))

        assert W_STAGES * W_ROWS * D <= F * D and W_SPLITS * W_ROWS * 2 * D <= F * D
        w_loads = v[1][:, 0, 0:W_STAGES * W_ROWS * D].rearrange("x (k r d) -> x k r d", r=W_ROWS, d=D)
        w_parts = v[1][:, 1, 0:W_SPLITS * W_ROWS * 2 * D].rearrange("x (k r h d) -> x k r h d", r=W_ROWS, h=2, d=D)

        identity_cleared = sem("identity_cleared")
        identity_ready = sem("identity_ready")
        w_loaded = [sem(f"w_loaded{k}") for k in range(W_STAGES)]
        w_hi_ready = sem("w_hi_ready")
        w_lo_ready = sem("w_lo_ready")
        v_loaded = [sem(f"v_loaded{b}") for b in range(2)]
        n_hi_ready = sem("n_hi_ready")
        n_lo_ready = sem("n_lo_ready")
        bank_turned = sem("bank_turned")
        bank_kept = sem("bank_kept")
        proj_ready = sem("proj_ready")
        product_ready = sem("product_ready")
        stored = [sem(f"stored{k}") for k in range(OUT_RING)]
        block = ctx.enter_context(nc.Block())

        def is_first(r, b):
            return isinstance(r, int) and r == 0 and b == 0

        def banks_before_field(r, b, i):
            if is_first(r, b):
                return W_TURNS * w_by[i] + i
            return (2 * r + b) * NF + W_TURNS * NW + i

        def cols(first, n):
            return slice(first * D, (first + n) * D)

        @block.sync
        def _(sp):
            def super_tile(r, b, last=False):
                s = 2 * r + b
                for c, gs in enumerate(chunks):
                    if is_first(r, b):
                        if c == load_at:
                            sp.wait_ge(bank_kept, banks_before_field(r, b, W_DONE))
                    elif c == 0 and not last:
                        sp.wait_ge(product_ready, s * NG)
                    if c == (load_at if is_first(r, b) else 0) and not last:
                        sp.dma_start(v[1 - b][:], emb_rows[s + 1]).then_inc(v_loaded[1 - b], 16)
                    first, n = first_pair[gs[0]], sum(sizes[g] for g in gs)
                    sp.wait_ge(product_ready, s * NG + gs[-1] + 1)
                    sp.dma_start(out_rows[s, :, :, cols(first, n)],
                                 out_chunk[:, c % OUT_RING, :, cols(0, n)]).then_inc(stored[c % OUT_RING], 16)

            load_at = next(c for c in range(NC) if groups[chunks[c][0]][0][0] >= W_DONE)
            sp.dma_start(v[0][:], emb_rows[0]).then_inc(v_loaded[0], 16)
            super_tile(0, 0)
            super_tile(0, 1)
            with sp.Fori(1, SUPER // 2 - 1) as r:
                super_tile(r, 0)
                super_tile(r, 1)
            super_tile(SUPER // 2 - 1, 0)
            super_tile(SUPER // 2 - 1, 1, last=True)
            for k in range(OUT_RING):
                sp.wait_ge(stored[k], 16 * SUPER * NC // OUT_RING)

        @block.tensor
        def _(pe):
            def turn(bank, blocks):
                for k, block_in in enumerate(blocks):
                    last = pe.transpose(turned[:, bank, k, :], block_in, identity[:])
                last.then_inc(bank_turned, 1)

            def turn_w(k):
                pe.wait_ge(w_lo_ready, k + 1)
                for n in range(W_TURNS):
                    before = W_TURNS * k + n + next(i for i in range(NF) if k < w_by[i])
                    if before >= T_RING:
                        pe.wait_ge(bank_kept, before - T_RING + 1)
                    turn(before % T_RING, [w_parts[:, k % W_SPLITS, m, :, :].rearrange("x h d -> x (h d)")
                                           for m in range(n * TURNS, (n + 1) * TURNS)])

            def turn_field(r, b, i):
                s = 2 * r + b
                if i % 2 == 0:
                    pe.wait_ge(n_lo_ready, s * NQ + i // 2 + 1)
                before = banks_before_field(r, b, i)
                if i >= T_RING or is_first(r, b):
                    pe.wait_ge(bank_kept, before - T_RING + 1)
                else:
                    pe.wait_ge(bank_kept, before - i - NF + last_user(i, T_RING, NF) + 1)
                turn(i % T_RING, [n_split[:, i // 2 % N_RING, t, i % 2, order * D:order * D + P].bitcast(F32)
                                  for order in range(2) for t in range(TILES)])

            def project(r, b, i):
                s = 2 * r + b
                pe.wait_ge(bank_kept, banks_before_field(r, b, i) + 1)
                for g in groups_of[i]:
                    if g >= UNITS:
                        pe.wait_ge(product_ready, s * NG + g - UNITS + 1)
                    elif not is_first(r, b):
                        pe.wait_ge(product_ready, s * NG - NG + last_user(g, UNITS, NG) + 1)
                    pair, at = first_pair[g], 0
                    for field, _, n in groups[g]:
                        for t in range(TILES):
                            for order in range(2):
                                last = pe.matmul(proj[:, g % UNITS, t, at:at + n * D],
                                                 s_split[:, field % S_RING, order * TILES + t, :],
                                                 w_split[:, cols(pair, n)], start=(order == 0), stop=(order == 1))
                        pair += n
                        at += n * D
                    last.then_inc(proj_ready, 1)

            def super_tile(r, b):
                for i in range(NF + AHEAD):
                    if is_first(r, b) and i < NF:
                        for k in w_before[i]:
                            turn_w(k)
                    if i < NF:
                        turn_field(r, b, i)
                    if i >= AHEAD:
                        project(r, b, i - AHEAD)

            pe.wait_ge(identity_ready, 1)
            super_tile(0, 0)
            super_tile(0, 1)
            with pe.Fori(1, SUPER // 2) as r:
                super_tile(r, 0)
                super_tile(r, 1)

        @block.scalar
        def _(act):
            def load_w(k):
                act.dma_start(w_loads[:, k % W_STAGES].rearrange("x r d -> x (r d)"),
                              w_rows[k]).then_inc(w_loaded[k % W_STAGES], 16)

            def w_hi(k):
                act.wait_ge(w_loaded[k % W_STAGES], 16 * (k // W_STAGES + 1))
                nc.scalar.copy(w_parts[:, k % W_SPLITS, :, 0, :].bitcast(F32R),
                               w_loads[:, k % W_STAGES]).then_inc(w_hi_ready, 1)

            def keep_w(k):
                chunk = w_split[:, cols(k * W_PAIRS, W_PAIRS)].rearrange("h (x m) -> h m x", m=W_ROWS)
                for n in range(W_TURNS):
                    before = W_TURNS * k + n + next(i for i in range(NF) if k < w_by[i])
                    act.wait_ge(bank_turned, before + 1)
                    nc.scalar.copy(chunk[:, n * TURNS:(n + 1) * TURNS, :],
                                   turned[:, before % T_RING]).then_inc(bank_kept, 1)

            def split_hi(r, b, q):
                if q == 0:
                    act.wait_ge(v_loaded[b], r * 16 + 16)
                if q >= N_RING:
                    act.wait_ge(bank_turned, banks_before_field(r, b, 2 * (q - N_RING) + 2))
                elif not is_first(r, b):
                    act.wait_ge(bank_turned, banks_before_field(r, b, min(2 * (q + NQ - N_RING) + 2, NF) - NF))
                fields = v[b][:, :, cols(2 * q, 2)].rearrange("p t (f d) -> p t f d", d=D)
                for at in (0, 2 * D):
                    nc.scalar.copy(n_split[:, q % N_RING, :, :, at:at + D], fields).then_inc(n_hi_ready, 1)

            def keep_field(r, b, i):
                s = 2 * r + b
                act.wait_ge(bank_turned, banks_before_field(r, b, i) + 1)
                if i >= S_RING:
                    act.wait_ge(proj_ready, s * NG + groups_through[i - S_RING])
                elif not is_first(r, b):
                    act.wait_ge(proj_ready, s * NG - NG + groups_through[last_user(i, S_RING, NF)])
                nc.scalar.copy(s_split[:, i % S_RING], turned[:, i % T_RING]).then_inc(bank_kept, 1)

            def super_tile(r, b):
                split_hi(r, b, 0)
                for i in range(NF):
                    if is_first(r, b):
                        for k in w_before[i]:
                            keep_w(k)
                            if k + W_SPLITS < NW:
                                w_hi(k + W_SPLITS)
                            if k + W_STAGES < NW:
                                act.wait_ge(w_lo_ready, k + 1)
                                load_w(k + W_STAGES)
                    if i % 2 == 0 and i // 2 + 1 < NQ:
                        split_hi(r, b, i // 2 + 1)
                    keep_field(r, b, i)

            for k in range(W_STAGES):
                load_w(k)
            for k in range(W_SPLITS):
                w_hi(k)
            super_tile(0, 0)
            super_tile(0, 1)
            with act.Fori(1, SUPER // 2) as r:
                super_tile(r, 0)
                super_tile(r, 1)

        @block.gpsimd
        def _(pool):
            nc.gpsimd.memset(identity[:], 0.0).then_inc(identity_cleared, 1)
            pool.wait_ge(identity_cleared, 1)
            nc.gpsimd.affine_select(out=identity[:], in_=identity[:], compare_op=ALU.not_equal, fill=1.0, base=0,
                                    pattern=[[-1, P]], channel_multiplier=1).then_inc(identity_ready, 1)

            def w_lo(k):
                pool.wait_ge(w_hi_ready, k + 1)
                parts = w_parts[:, k % W_SPLITS]
                nc.gpsimd.tensor_tensor(parts[:, :, 1, :], w_loads[:, k % W_STAGES], parts[:, :, 0, :],
                                        ALU.subtract).then_inc(w_lo_ready, 1)

            def split_lo(r, b, q):
                pool.wait_ge(n_hi_ready, 2 * ((2 * r + b) * NQ + q + 1))
                fields = v[b][:, :, cols(2 * q, 2)].rearrange("p t (f d) -> p t f d", d=D)
                parts = n_split[:, q % N_RING]
                nc.gpsimd.tensor_tensor(parts[:, :, :, D:2 * D], fields, parts[:, :, :, 0:D].bitcast(F32),
                                        ALU.subtract).then_inc(n_lo_ready, 1)

            def super_tile(r, b):
                split_lo(r, b, 0)
                for i in range(NF):
                    if is_first(r, b):
                        for k in w_before[i]:
                            if k + W_SPLITS < NW:
                                w_lo(k + W_SPLITS)
                    if i % 2 == 0 and i // 2 + 1 < NQ:
                        split_lo(r, b, i // 2 + 1)

            for k in range(W_SPLITS):
                w_lo(k)
            super_tile(0, 0)
            super_tile(0, 1)
            with pool.Fori(1, SUPER // 2) as r:
                super_tile(r, 0)
                super_tile(r, 1)

        @block.vector
        def _(dve):
            def super_tile(r, b):
                s = 2 * r + b
                for g in range(NG):
                    c = chunk_of[g]
                    if g == chunks[c][0] and (not is_first(r, b) or c >= OUT_RING):
                        dve.wait_ge(stored[c % OUT_RING], (s * (NC // OUT_RING) + c // OUT_RING) * 16)
                    dve.wait_ge(proj_ready, s * NG + g + 1)
                    to = (first_pair[g] - first_pair[chunks[c][0]]) * D
                    at = 0
                    for _, j, n in groups[g]:
                        last = nc.vector.tensor_tensor(out_chunk[:, c % OUT_RING, :, to:to + n * D],
                                                       proj[:, g % UNITS, :, at:at + n * D],
                                                       v[b][:, :, cols(j, n)], ALU.mult)
                        to += n * D
                        at += n * D
                    last.then_inc(product_ready, 1)

            super_tile(0, 0)
            super_tile(0, 1)
            with dve.Fori(1, SUPER // 2) as r:
                super_tile(r, 0)
                super_tile(r, 1)


def kernel(r_feature_emb, L0_rec_W):
    import numpy as np
    import concourse.bacc as bacc
    from concourse.bass_utils import run_bass_kernel_spmd

    nc = bacc.Bacc("TRN2", target_bir_lowering=False, num_devices=1)
    arrays = {"emb_dram": np.ascontiguousarray(r_feature_emb), "w_dram": np.ascontiguousarray(L0_rec_W)}
    ins = [nc.dram_tensor(name, a.shape, mybir.dt.from_np(a.dtype), kind="ExternalInput").ap()
           for name, a in arrays.items()]
    B, _, D = r_feature_emb.shape
    out = nc.dram_tensor("out_dram", (B, L0_rec_W.shape[0], D), F32, kind="ExternalOutput").ap()
    bilinear_interaction(nc, *ins, out)
    return run_bass_kernel_spmd(nc, [arrays], core_ids=[0]).results[0]["out_dram"]
```

```python
from contextlib import ExitStack
from math import ceil

import concourse.bass as bass
from concourse import mybir

ALU = mybir.AluOpType
F32 = mybir.dt.float32
F32R = mybir.dt.float32r

P = 128
TILES = 2
BANK = 512
UNITS = 3
N_RING = 2
T_RING = 2
S_RING = 4
AHEAD = 2
RELIEF_EVERY = 6
OUT_RING = 4
OUT_PAIRS = 16
W_ROWS = 8
W_STAGES = 4
W_SPLITS = 2
W_FIRST = 2
W_RATE = 0.7


def cut_groups(fields, bank_pairs):
    groups = []
    for i in range(fields - 1):
        left = fields - 1 - i
        if left == 1:
            groups[-1].append((i, i + 1, 1))
            continue
        n, j = ceil(left / bank_pairs), i + 1
        for k in range(n):
            size = left // n + (k < left % n)
            groups.append([(i, j, size)])
            j += size
    return groups


def cut_chunks(sizes, most):
    chunks, held = [[]], 0
    for g, size in enumerate(sizes):
        if held + size > most:
            chunks.append([])
            held = 0
        chunks[-1].append(g)
        held += size
    return chunks


def last_user(k, ring, count):
    return max(n for n in range(count) if n % ring == k % ring)


def bilinear_interaction(nc, emb, w, out):
    B, F, D = emb.shape
    NP = w.shape[0]
    SUPER = B // (TILES * P)
    NF = F - 1
    NQ = F // 2
    groups = cut_groups(F, BANK // D)
    NG = len(groups)
    sizes = [sum(n for _, _, n in g) for g in groups]
    first_pair = [sum(sizes[:g]) for g in range(NG)]
    chunks = cut_chunks(sizes, OUT_PAIRS)
    NC = len(chunks)
    chunk_of = {g: c for c, gs in enumerate(chunks) for g in gs}
    groups_of = [[g for g in range(NG) if groups[g][-1][0] == i] for i in range(NF)]
    groups_through = [sum(g[0][0] <= i for g in groups) for i in range(NF)]

    W_PAIRS = W_ROWS * P // D
    NW = NP // W_PAIRS
    W_TURNS = W_ROWS * P // BANK
    TURNS = BANK // P
    first_order, later_order, n_w, n_f = [], [], 0, 0
    for i in range(NF):
        later_order += [("f", i + AHEAD)] + [("g", g) for g in groups_of[i]]
        for g in groups_of[i]:
            w_want = min(NW, max(ceil((first_pair[g] + sizes[g]) / W_PAIRS), ceil(W_RATE * (g + 1)), W_FIRST))
            f_want = i + 1 + min(g, AHEAD)
            first_order += [("w", k) for k in range(n_w, w_want) if k == 0 or g > 0]
            first_order += [("f", k) for k in range(n_f, f_want)]
            first_order += [("w", k) for k in range(n_w, w_want) if k > 0 and g == 0]
            first_order.append(("g", g))
            n_w, n_f = w_want, f_want
    banks_before, turns = {}, 0
    for item in first_order:
        banks_before[item] = turns
        turns += {"w": W_TURNS, "f": 1, "g": 0}[item[0]]
    w_done = first_order.index(("w", NW - 1))
    by_pool = [g for g in range(NG) if g % RELIEF_EVERY == RELIEF_EVERY - 2 and groups[g][0][0] < NF - 8]
    assert all(sum(g in by_pool for g in gs) <= 1 < len(gs) for gs in chunks if set(gs) & set(by_pool))
    NR = len(by_pool)

    assert NP == F * (F - 1) // 2 and 2 * D == P and B % (2 * TILES * P) == 0 and SUPER >= 4
    assert NC % OUT_RING == 0 and NF % 2 == 1 and NQ % N_RING == 0 and 2 * TILES == TURNS
    assert T_RING == 2 and W_TURNS % 2 == 0 and NP % W_PAIRS == 0 and banks_before[("f", NF)] == W_TURNS * NW + NF
    assert n_f == NF + AHEAD and n_w == NW and W_SPLITS <= W_STAGES < NW

    V_FIRST = [(0, 2), (2, 9), (9, 17), (17, F)]

    emb_rows = emb.rearrange("(s t p) f d -> s p t (f d)", t=TILES, p=P)
    out_rows = out.rearrange("(s t p) n e -> s p t (n e)", t=TILES, p=P)
    w_rows = w.rearrange("n e d -> (n e d)").rearrange("(k x m) -> k x m", x=P, m=W_ROWS * D)

    with ExitStack() as ctx:
        def sb(name, shape, dt=F32):
            return ctx.enter_context(nc.sbuf_tensor(name, shape, dt))

        def sem(name):
            return ctx.enter_context(nc.semaphore(name))

        w_split = sb("w_split", [P, NP * D], F32R)
        v = [sb(f"v{b}", [P, TILES, F * D]) for b in range(2)]
        n_split = sb("n_split", [P, N_RING, TILES, 2, 3 * D], F32R)
        s_split = sb("s_split", [P, S_RING, 2 * TILES, P], F32R)
        out_chunk = sb("out_chunk", [P, OUT_RING, TILES, OUT_PAIRS * D])
        identity = sb("identity", [P, P])
        proj = ctx.enter_context(nc.psum_tensor("proj", [P, UNITS, TILES, BANK], F32))
        turned = ctx.enter_context(nc.psum_tensor("turned", [P, T_RING, TURNS, P], F32))

        assert W_STAGES * W_ROWS * D <= F * D and W_SPLITS * W_ROWS * 2 * D <= F * D
        w_loads = v[1][:, 0, 0:W_STAGES * W_ROWS * D].rearrange("x (k r d) -> x k r d", r=W_ROWS, d=D)
        w_parts = v[1][:, 1, 0:W_SPLITS * W_ROWS * 2 * D].rearrange("x (k r h d) -> x k r h d", r=W_ROWS, h=2, d=D)

        identity_cleared = sem("identity_cleared")
        identity_ready = sem("identity_ready")
        w_loaded = [sem(f"w_loaded{k}") for k in range(W_STAGES)]
        w_hi_ready = sem("w_hi_ready")
        w_lo_ready = sem("w_lo_ready")
        v_first_loaded = [sem(f"v_first_loaded{k}") for k in range(len(V_FIRST))]
        v_loaded = [sem(f"v_loaded{b}") for b in range(2)]
        n_hi_ready = sem("n_hi_ready")
        n_lo_ready = sem("n_lo_ready")
        bank_turned = sem("bank_turned")
        bank_kept = sem("bank_kept")
        proj_ready = sem("proj_ready")
        product_ready = sem("product_ready")
        relief_copied = sem("relief_copied")
        relief_ready = sem("relief_ready")
        stored = [sem(f"stored{k}") for k in range(OUT_RING)]
        block = ctx.enter_context(nc.Block())

        def is_first(r, b):
            return isinstance(r, int) and r == 0 and b == 0

        def following(r, b):
            return (r, 1) if b == 0 else (r + 1, 0)

        def tile_and_field(r, b, i):
            return (r, b, i) if i < NF else (*following(r, b), i - NF)

        def order(r, b, last):
            return [(kind, n) for kind, n in (first_order if is_first(r, b) else later_order)
                    if not (last and kind == "f" and n >= NF)]

        def banks_before_field(r, b, i):
            if is_first(r, b):
                return banks_before[("f", i)]
            return (2 * r + b) * NF + W_TURNS * NW + i

        def before(r, b):
            return (r, 0) if b == 1 else (r - 1, 1)

        def relieved(r, b, g):
            return g in by_pool and not is_first(r, b)

        def products_before(r, b, g):
            if is_first(r, b):
                return g, 0
            on_pool = sum(n < g for n in by_pool)
            return (2 * r + b) * (NG - NR) + NR + g - on_pool, (2 * r + b - 1) * NR + on_pool

        def wait_chunk_filled(eng, r, b, c):
            on_dve, on_pool = products_before(r, b, chunks[c][-1] + 1)
            if any(relieved(r, b, g) for g in chunks[c]):
                eng.wait_ge(relief_ready, on_pool)
            else:
                eng.wait_ge(product_ready, on_dve)

        def wait_chunk_free(eng, r, b, c):
            if not is_first(r, b) or c >= OUT_RING:
                eng.wait_ge(stored[c % OUT_RING], ((2 * r + b) * (NC // OUT_RING) + c // OUT_RING) * 16)

        def in_chunk(g):
            first = first_pair[chunks[chunk_of[g]][0]]
            return cols(first_pair[g] - first, sizes[g])

        def load_w(eng, k):
            eng.dma_start(w_loads[:, k % W_STAGES].rearrange("x r d -> x (r d)"),
                          w_rows[k]).then_inc(w_loaded[k % W_STAGES], 16)

        def wait_v_first(eng, field, waited):
            for k, (a, b) in enumerate(V_FIRST):
                if k not in waited and a <= field:
                    eng.wait_ge(v_first_loaded[k], 16)
                    waited.add(k)

        def cols(first, n):
            return slice(first * D, (first + n) * D)

        @block.sync
        def _(sp):
            load_at = next(c for c in range(NC) if first_order.index(("g", chunks[c][0])) > w_done)

            def super_tile(r, b, last=False):
                s = 2 * r + b
                for c, gs in enumerate(chunks):
                    if c == (load_at if is_first(r, b) else 0) and not last:
                        if is_first(r, b):
                            sp.wait_ge(bank_kept, banks_before[("w", NW - 1)] + W_TURNS)
                        sp.dma_start(v[1 - b][:], emb_rows[s + 1]).then_inc(v_loaded[1 - b], 16)
                    wait_chunk_filled(sp, r, b, c)
                    n = sum(sizes[g] for g in gs)
                    sp.dma_start(out_rows[s, :, :, cols(first_pair[gs[0]], n)],
                                 out_chunk[:, c % OUT_RING, :, cols(0, n)]).then_inc(stored[c % OUT_RING], 16)

            assert len(V_FIRST) == W_STAGES
            for k, (a, b) in enumerate(V_FIRST):
                load_w(sp, k)
                sp.dma_start(v[0][:, :, cols(a, b - a)],
                             emb_rows[0][:, :, cols(a, b - a)]).then_inc(v_first_loaded[k], 16)
            super_tile(0, 0)
            super_tile(0, 1)
            with sp.Fori(1, SUPER // 2 - 1) as r:
                super_tile(r, 0)
                super_tile(r, 1)
            super_tile(SUPER // 2 - 1, 0)
            super_tile(SUPER // 2 - 1, 1, last=True)
            for k in range(OUT_RING):
                sp.wait_ge(stored[k], 16 * SUPER * NC // OUT_RING)

        @block.tensor
        def _(pe):
            def turn(bank, blocks):
                for k, block_in in enumerate(blocks):
                    last = pe.transpose(turned[:, bank, k, :], block_in, identity[:])
                last.then_inc(bank_turned, 1)

            def turn_w(k):
                pe.wait_ge(w_lo_ready, k + 1)
                for n in range(W_TURNS):
                    before = banks_before[("w", k)] + n
                    if before >= T_RING:
                        pe.wait_ge(bank_kept, before - T_RING + 1)
                    turn(before % T_RING, [w_parts[:, k % W_SPLITS, m, :, :].rearrange("x h d -> x (h d)")
                                           for m in range(n * TURNS, (n + 1) * TURNS)])

            def turn_field(r, b, i):
                s = 2 * r + b
                if i % 2 == 0:
                    pe.wait_ge(n_lo_ready, s * NQ + i // 2 + 1)
                before = banks_before_field(r, b, i)
                if i >= T_RING or is_first(r, b):
                    if not is_first(r, b) or before >= T_RING:
                        pe.wait_ge(bank_kept, before - T_RING + 1)
                else:
                    pe.wait_ge(bank_kept, before - i - NF + last_user(i, T_RING, NF) + 1)
                turn(i % T_RING, [n_split[:, i // 2 % N_RING, t, i % 2, order * D:order * D + P].bitcast(F32)
                                  for order in range(2) for t in range(TILES)])

            def project(r, b, g):
                s = 2 * r + b
                kept = banks_before_field(r, b, groups[g][-1][0]) + 1
                if is_first(r, b):
                    w_last = ceil((first_pair[g] + sizes[g]) / W_PAIRS) - 1
                    kept = max(kept, banks_before[("w", w_last)] + W_TURNS)
                pe.wait_ge(bank_kept, kept)
                if g >= UNITS or not is_first(r, b):
                    user = (r, b, g - UNITS) if g >= UNITS else (*before(r, b), last_user(g, UNITS, NG))
                    on_dve, on_pool = products_before(*user)
                    if relieved(*user):
                        pe.wait_ge(relief_copied, on_pool + 1)
                    else:
                        pe.wait_ge(product_ready, on_dve + 1)
                pair, at = first_pair[g], 0
                for field, _, n in groups[g]:
                    for t in range(TILES):
                        for order in range(2):
                            last = pe.matmul(proj[:, g % UNITS, t, at:at + n * D],
                                             s_split[:, field % S_RING, order * TILES + t, :],
                                             w_split[:, cols(pair, n)], start=(order == 0), stop=(order == 1))
                    pair += n
                    at += n * D
                last.then_inc(proj_ready, 1)

            def super_tile(r, b, last=False):
                for kind, n in order(r, b, last):
                    if kind == "w":
                        turn_w(n)
                    elif kind == "f":
                        turn_field(*tile_and_field(r, b, n))
                    else:
                        project(r, b, n)

            pe.wait_ge(identity_ready, 1)
            super_tile(0, 0)
            super_tile(0, 1)
            with pe.Fori(1, SUPER // 2 - 1) as r:
                super_tile(r, 0)
                super_tile(r, 1)
            super_tile(SUPER // 2 - 1, 0)
            super_tile(SUPER // 2 - 1, 1, last=True)

        @block.scalar
        def _(act):
            waited = set()

            def w_hi(k):
                act.wait_ge(w_loaded[k % W_STAGES], 16 * (k // W_STAGES + 1))
                nc.scalar.copy(w_parts[:, k % W_SPLITS, :, 0, :].bitcast(F32R),
                               w_loads[:, k % W_STAGES]).then_inc(w_hi_ready, 1)

            def keep_w(k):
                chunk = w_split[:, cols(k * W_PAIRS, W_PAIRS)].rearrange("h (x m) -> h m x", m=W_ROWS)
                for n in range(W_TURNS):
                    before = banks_before[("w", k)] + n
                    act.wait_ge(bank_turned, before + 1)
                    nc.scalar.copy(chunk[:, n * TURNS:(n + 1) * TURNS, :],
                                   turned[:, before % T_RING]).then_inc(bank_kept, 1)

            def split_hi(r, b, q):
                if is_first(r, b):
                    wait_v_first(act, 2 * q + 1, waited)
                elif q == 0:
                    act.wait_ge(v_loaded[b], (r + b) * 16)
                if q >= N_RING:
                    act.wait_ge(bank_turned, banks_before_field(r, b, 2 * (q - N_RING) + 2))
                elif not is_first(r, b):
                    act.wait_ge(bank_turned, banks_before_field(r, b, min(2 * (q + NQ - N_RING) + 2, NF) - NF))
                fields = v[b][:, :, cols(2 * q, 2)].rearrange("p t (f d) -> p t f d", d=D)
                for at in (0, 2 * D):
                    nc.scalar.copy(n_split[:, q % N_RING, :, :, at:at + D], fields).then_inc(n_hi_ready, 1)

            def keep_field(r, b, i):
                s = 2 * r + b
                act.wait_ge(bank_turned, banks_before_field(r, b, i) + 1)
                if i >= S_RING:
                    act.wait_ge(proj_ready, s * NG + groups_through[i - S_RING])
                elif not is_first(r, b):
                    act.wait_ge(proj_ready, s * NG - NG + groups_through[last_user(i, S_RING, NF)])
                nc.scalar.copy(s_split[:, i % S_RING], turned[:, i % T_RING]).then_inc(bank_kept, 1)

            def relieve(r, b, g):
                wait_chunk_free(act, r, b, chunk_of[g])
                act.wait_ge(proj_ready, (2 * r + b) * NG + g + 1)
                nc.scalar.copy(out_chunk[:, chunk_of[g] % OUT_RING, :, in_chunk(g)],
                               proj[:, g % UNITS, :, 0:sizes[g] * D]).then_inc(relief_copied, 1)

            def super_tile(r, b, last=False):
                for kind, n in order(r, b, last):
                    if kind == "w":
                        keep_w(n)
                        if n + W_SPLITS < NW:
                            w_hi(n + W_SPLITS)
                        if n + W_STAGES < NW:
                            act.wait_ge(w_lo_ready, n + 1)
                            load_w(act, n + W_STAGES)
                    elif kind == "f":
                        at, tb, i = tile_and_field(r, b, n)
                        if is_first(at, tb) and i == 0:
                            keep_field(at, tb, i)
                            split_hi(at, tb, 1)
                            continue
                        if i % 2 == 0 and i // 2 + 1 < NQ:
                            split_hi(at, tb, i // 2 + 1)
                        elif i == NF - 1 and not last:
                            split_hi(*following(at, tb), 0)
                        keep_field(at, tb, i)
                    elif relieved(r, b, n):
                        relieve(r, b, n)

            w_hi(0)
            split_hi(0, 0, 0)
            w_hi(1)
            super_tile(0, 0)
            super_tile(0, 1)
            with act.Fori(1, SUPER // 2 - 1) as r:
                super_tile(r, 0)
                super_tile(r, 1)
            super_tile(SUPER // 2 - 1, 0)
            super_tile(SUPER // 2 - 1, 1, last=True)

        @block.gpsimd
        def _(pool):
            nc.gpsimd.memset(identity[:], 0.0).then_inc(identity_cleared, 1)
            pool.wait_ge(identity_cleared, 1)
            nc.gpsimd.affine_select(out=identity[:], in_=identity[:], compare_op=ALU.not_equal, fill=1.0, base=0,
                                    pattern=[[-1, P]], channel_multiplier=1).then_inc(identity_ready, 1)

            def w_lo(k):
                pool.wait_ge(w_hi_ready, k + 1)
                parts = w_parts[:, k % W_SPLITS]
                nc.gpsimd.tensor_tensor(parts[:, :, 1, :], w_loads[:, k % W_STAGES], parts[:, :, 0, :],
                                        ALU.subtract).then_inc(w_lo_ready, 1)

            def split_lo(r, b, q):
                pool.wait_ge(n_hi_ready, 2 * ((2 * r + b) * NQ + q + 1))
                fields = v[b][:, :, cols(2 * q, 2)].rearrange("p t (f d) -> p t f d", d=D)
                parts = n_split[:, q % N_RING]
                nc.gpsimd.tensor_tensor(parts[:, :, :, D:2 * D], fields, parts[:, :, :, 0:D].bitcast(F32),
                                        ALU.subtract).then_inc(n_lo_ready, 1)

            def multiply(r, b, g):
                pool.wait_ge(relief_copied, products_before(r, b, g)[1] + 1)
                pool.wait_ge(product_ready, products_before(r, b, chunks[chunk_of[g]][-1] + 1)[0])
                (_, j, n), = groups[g]
                chunk = out_chunk[:, chunk_of[g] % OUT_RING, :, in_chunk(g)]
                nc.gpsimd.tensor_tensor(chunk, chunk, v[b][:, :, cols(j, n)], ALU.mult).then_inc(relief_ready, 1)

            def super_tile(r, b, last=False):
                for kind, n in order(r, b, last):
                    if kind == "w" and n + W_SPLITS < NW:
                        w_lo(n + W_SPLITS)
                    elif kind == "f":
                        at, tb, i = tile_and_field(r, b, n)
                        if i % 2 == 0 and i // 2 + 1 < NQ:
                            split_lo(at, tb, i // 2 + 1)
                        elif i == NF - 1 and not last:
                            split_lo(*following(at, tb), 0)
                    elif kind == "g" and relieved(r, b, n):
                        multiply(r, b, n)

            w_lo(0)
            split_lo(0, 0, 0)
            w_lo(1)
            super_tile(0, 0)
            super_tile(0, 1)
            with pool.Fori(1, SUPER // 2 - 1) as r:
                super_tile(r, 0)
                super_tile(r, 1)
            super_tile(SUPER // 2 - 1, 0)
            super_tile(SUPER // 2 - 1, 1, last=True)

        @block.vector
        def _(dve):
            waited = set()

            def super_tile(r, b):
                s = 2 * r + b
                for g in range(NG):
                    if relieved(r, b, g):
                        continue
                    c = chunk_of[g]
                    if g == min(n for n in chunks[c] if not relieved(r, b, n)):
                        wait_chunk_free(dve, r, b, c)
                    dve.wait_ge(proj_ready, s * NG + g + 1)
                    if is_first(r, b):
                        wait_v_first(dve, groups[g][0][1] + groups[g][0][2] - 1, waited)
                    to = (first_pair[g] - first_pair[chunks[c][0]]) * D
                    at = 0
                    for _, j, n in groups[g]:
                        last = nc.vector.tensor_tensor(out_chunk[:, c % OUT_RING, :, to:to + n * D],
                                                       proj[:, g % UNITS, :, at:at + n * D],
                                                       v[b][:, :, cols(j, n)], ALU.mult)
                        to += n * D
                        at += n * D
                    last.then_inc(product_ready, 1)

            super_tile(0, 0)
            super_tile(0, 1)
            with dve.Fori(1, SUPER // 2) as r:
                super_tile(r, 0)
                super_tile(r, 1)


def kernel(r_feature_emb, L0_rec_W):
    import numpy as np
    import concourse.bacc as bacc
    from concourse.bass_utils import run_bass_kernel_spmd

    nc = bacc.Bacc("TRN2", target_bir_lowering=False, num_devices=1)
    arrays = {"emb_dram": np.ascontiguousarray(r_feature_emb), "w_dram": np.ascontiguousarray(L0_rec_W)}
    ins = [nc.dram_tensor(name, a.shape, mybir.dt.from_np(a.dtype), kind="ExternalInput").ap()
           for name, a in arrays.items()]
    B, _, D = r_feature_emb.shape
    out = nc.dram_tensor("out_dram", (B, L0_rec_W.shape[0], D), F32, kind="ExternalOutput").ap()
    bilinear_interaction(nc, *ins, out)
    return run_bass_kernel_spmd(nc, [arrays], core_ids=[0]).results[0]["out_dram"]
```
